# Optimizing a Trainium2 kernel written in Bass

```python
import numpy as np
import jax
import jax.numpy as jnp

def _softmax(x, axis=-1):
    return jax.nn.softmax(x, axis=axis)

def _gelu(x):
    return jax.nn.gelu(x, approximate=True)

def _silu(x):
    return jax.nn.silu(x)

def _sigmoid(x):
    return jax.nn.sigmoid(x)

def _layernorm(x, axis=-1, eps=1e-05):
    m = jnp.mean(x, axis=axis, keepdims=True)
    v = jnp.var(x, axis=axis, keepdims=True)
    return (x - m) / jnp.sqrt(v + eps)

def _scatter_add(tgt, idx, src, axis=0):
    return tgt.at[idx].add(src)

def _segment_sum(src, seg, n):
    return jax.ops.segment_sum(src, seg, n)
kernel_name = 'mk_gnn_ffn_d1_gnn_r8_d3c4bd'

def setup_inputs(seed: int=0):
    np.random.seed(seed)
    _w = jnp.asarray

    def _rec_inputs():
        import jax
        import jax.numpy as jnp
        _gk = jax.random.key(seed)
        x = -0.0002117 + 1 * jax.random.normal(jax.random.fold_in(_gk, 1), (6250, 256), jnp.float32)
        src = jax.random.randint(jax.random.fold_in(_gk, 2), (100000,), 0, 6250, jnp.int32)
        dst = jnp.minimum((6250 * jax.random.uniform(jax.random.fold_in(_gk, 3), (100000,)) ** 2.0).astype(jnp.int32), 49999)
        _o = jnp.argsort(dst, stable=True)
        src = src[_o]
        dst = dst[_o]
        edge_weight = jax.random.uniform(jax.random.fold_in(_gk, 12), (100000,), jnp.float32, 0.0, 1)
        return (x, src, dst, edge_weight)
    x, src, dst, edge_weight = _rec_inputs()

    def _L0_gnn_setup():
        import jax, jax.numpy as jnp
        import numpy as np
        N_NODES = 12500
        N_EDGES = 400000
        D_IN = 256
        D_OUT = 256
        key = jax.random.key(seed)
        k1, k2, k3, k4, k5 = jax.random.split(key, 5)
        inputs = jax.random.normal(k1, (N_NODES, D_IN), dtype=jnp.float32)
        init_range = np.sqrt(6.0 / (D_IN + D_OUT)).astype(np.float32)
        weight = jax.random.uniform(k2, (D_IN, D_OUT), dtype=jnp.float32, minval=-init_range, maxval=init_range)
        edge_src = jax.random.randint(k3, (N_EDGES,), 0, N_NODES, dtype=jnp.int32)
        edge_dst = jax.random.randint(k4, (N_EDGES,), 0, N_NODES, dtype=jnp.int32)
        edge_vals = jax.random.uniform(k5, (N_EDGES,), dtype=jnp.float32)
        return {'inputs': inputs, 'weight': weight, 'edge_src': edge_src, 'edge_dst': edge_dst, 'edge_vals': edge_vals}
    _L0_gnn_all = _L0_gnn_setup()
    _L0_gnn_in = {k: v for k, v in _L0_gnn_all.items() if k in ('weight',)}
    del _L0_gnn_all

    def _L0_ffn_setup():
        import math
        import jax, jax.numpy as jnp
        import numpy as np
        CAPACITY_FACTOR = 1.25
        TOP_K = 2
        LN_EPS = 1e-05

        def _layer_norm(x, gamma, beta):
            mu = jnp.mean(x, axis=-1, keepdims=True)
            var = jnp.var(x, axis=-1, keepdims=True)
            return (x - mu) * jax.lax.rsqrt(var + LN_EPS) * gamma + beta
        key = jax.random.key(seed)
        ks = jax.random.split(key, 4)
        B, S, D, F, E = (8, 512, 256, 512, 8)
        x = jax.random.normal(ks[0], (B, S, D), dtype=jnp.float32)
        Wr = jax.random.normal(ks[1], (D, E), dtype=jnp.float32) / np.sqrt(D)
        br = jnp.zeros((E,), jnp.float32)
        W1 = jax.random.normal(ks[2], (E, D, F), dtype=jnp.float32) / np.sqrt(D)
        b1 = jnp.zeros((E, F), jnp.float32)
        W2 = jax.random.normal(ks[3], (E, F, D), dtype=jnp.float32) / np.sqrt(F)
        b2 = jnp.zeros((E, D), jnp.float32)
        gamma = jnp.ones((D,), jnp.float32)
        beta = jnp.zeros((D,), jnp.float32)
        return {'x': x, 'Wr': Wr, 'br': br, 'W1': W1, 'b1': b1, 'W2': W2, 'b2': b2, 'gamma': gamma, 'beta': beta}
    _L0_ffn_all = _L0_ffn_setup()
    _L0_ffn_in = {k: v for k, v in _L0_ffn_all.items() if k in ('Wr', 'br', 'W1', 'b1', 'W2', 'b2', 'gamma', 'beta')}
    del _L0_ffn_all
    return {'x': x, 'src': src, 'dst': dst, 'edge_weight': edge_weight, 'L0_gnn_weight': _L0_gnn_in['weight'], 'L0_ffn_Wr': _L0_ffn_in['Wr'], 'L0_ffn_br': _L0_ffn_in['br'], 'L0_ffn_W1': _L0_ffn_in['W1'], 'L0_ffn_b1': _L0_ffn_in['b1'], 'L0_ffn_W2': _L0_ffn_in['W2'], 'L0_ffn_b2': _L0_ffn_in['b2'], 'L0_ffn_gamma': _L0_ffn_in['gamma'], 'L0_ffn_beta': _L0_ffn_in['beta']}

def reference(x, src, dst, edge_weight, L0_gnn_weight, L0_ffn_Wr, L0_ffn_br, L0_ffn_W1, L0_ffn_b1, L0_ffn_W2, L0_ffn_b2, L0_ffn_gamma, L0_ffn_beta):
    import jax
    import jax.numpy as jnp

    def _L0_gnn_ref(inputs, weight, edge_src, edge_dst, edge_vals):
        import jax, jax.numpy as jnp
        import numpy as np
        N_NODES = 12500
        N_EDGES = 400000
        D_IN = 256
        D_OUT = 256
        x = inputs @ weight
        msgs = edge_vals[:, None] * x[edge_src]
        out = jax.ops.segment_sum(msgs, edge_dst, num_segments=inputs.shape[0])
        return jax.nn.relu(out)

    def _L0_ffn_ref(x, Wr, br, W1, b1, W2, b2, gamma, beta):
        import math
        import jax, jax.numpy as jnp
        import numpy as np
        CAPACITY_FACTOR = 1.25
        TOP_K = 2
        LN_EPS = 1e-05

        def _layer_norm(x, gamma, beta):
            mu = jnp.mean(x, axis=-1, keepdims=True)
            var = jnp.var(x, axis=-1, keepdims=True)
            return (x - mu) * jax.lax.rsqrt(var + LN_EPS) * gamma + beta
        B, S, D = x.shape
        E = Wr.shape[1]
        N = B * S
        K = TOP_K
        logits = jnp.mean(x, axis=1) @ Wr + br
        routing_weights = jax.nn.softmax(logits, axis=-1)
        capacity = float(math.ceil(N * CAPACITY_FACTOR / E))
        expected_loads = routing_weights.sum(axis=0) * (N / B)
        scale = jnp.where(expected_loads > capacity, capacity / expected_loads, 1.0)
        routing_weights = jax.nn.softmax(routing_weights * scale, axis=-1)
        rw_tok = jnp.broadcast_to(routing_weights[:, None, :], (B, S, E)).reshape(N, E)
        top_w, top_i = jax.lax.top_k(rw_tok, K)
        top_w = jax.nn.softmax(top_w, axis=-1)
        xf = x.reshape(N, D)
        h = jax.nn.gelu(jnp.einsum('nd,edf->enf', xf, W1) + b1[:, None, :], approximate=False)
        y = jnp.einsum('enf,efd->end', h, W2) + b2[:, None, :]
        w_dense = jnp.zeros((N, E), x.dtype).at[jnp.arange(N)[:, None], top_i].add(top_w)
        out = jnp.einsum('ne,end->nd', w_dense, y).reshape(B, S, D)
        out = _layer_norm(out + x, gamma, beta)
        return out
    x = x + _L0_gnn_ref(_layernorm(x, axis=-1), L0_gnn_weight, src, dst, edge_weight)
    x = x + _L0_ffn_ref(_layernorm(x, axis=-1)[None], L0_ffn_Wr, L0_ffn_br, L0_ffn_W1, L0_ffn_b1, L0_ffn_W2, L0_ffn_b2, L0_ffn_gamma, L0_ffn_beta)[0]
    return x

_drawn_inputs = setup_inputs


def setup_inputs(seed=0):
    import zlib

    import numpy as np

    out = dict(_drawn_inputs(seed))
    spreads = {'L0_ffn_br': (0.0, 0.1),
     'L0_ffn_b1': (0.0, 0.523),
     'L0_ffn_b2': (0.0, 0.352),
     'L0_ffn_gamma': (1.0, 0.2),
     'L0_ffn_beta': (0.0, 0.1)}
    factors = {'L0_ffn_Wr': 8.0}
    for name, (base, spread) in spreads.items():
        noise = np.random.default_rng([zlib.crc32(name.encode()), seed]).standard_normal(out[name].shape)
        drawn = base * np.exp(spread * noise) if base else spread * noise
        out[name] = jnp.asarray(drawn.astype(out[name].dtype))
    for name, factor in factors.items():
        out[name] = (out[name] * factor).astype(out[name].dtype)
    return out
```

```python
import concourse.bass as bass
from concourse import mybir
from contextlib import ExitStack

F32 = mybir.dt.float32
F32R = mybir.dt.float32r
I32 = mybir.dt.int32
U32 = mybir.dt.uint32
ALU = mybir.AluOpType
ACT = mybir.ActivationFunctionType
AX = mybir.AxisListType

P = 128
NODES, D, EDGES = 6250, 256, 100000
FF, EXPERTS, TOPK = 512, 8, 2
KD = D // P
KF = FF // P
EPS = 1e-5
CAPACITY = float(-(-NODES * 5 // (4 * EXPERTS)))

GROUP, GROUPS = 2, 4
HALF = GROUP * GROUPS
ITER = 2 * HALF
FULL = EDGES // P
LEFT = EDGES - FULL * P
ITERS = -(-(FULL + 1) // ITER)
TILES = ITERS * ITER
ROWCH = FULL // P
ROWREST = FULL - ROWCH * P
ROWTAIL = TILES - ROWCH * P
WIN = 64
WIDE = 512
WIDES = -(-NODES // WIDE)
COLS = WIDES * WIDE

CH = 2
CHW = CH * P
CHUNKS = -(-NODES // CHW)
NT = CHUNKS * CH
NFULL = NODES // P
NREST = NODES - NFULL * P
HT = TOPK * KF
PAIRS = HT // 2


def gnn_moe(nc, x, src, dst, edge_w, gnn_w, wr, br, w1, b1, w2, b2, gamma, beta, out):
    ctx = ExitStack()
    with ctx:
        def sb(name, shape, dt, stack=ctx):
            return stack.enter_context(nc.sbuf_tensor(name, shape, dt))

        def sem(name):
            return ctx.enter_context(nc.semaphore(name))

        aggT = sb("aggT", [P, KD, COLS], F32)
        x1 = sb("x1", [P, NT, D], F32)
        gnnw_sb = sb("gnnw_sb", [P, KD, D], F32)
        ident = sb("ident", [P, P], F32)
        ones = sb("ones", [P, P], F32)
        epsc = sb("epsc", [P, 1], F32)
        rstd1 = sb("rstd1", [P, NT], F32)
        shift1 = sb("shift1", [P, NT], F32)
        gamma_bc = sb("gamma_bc", [P, D], F32)
        beta_bc = sb("beta_bc", [P, D], F32)
        wr_sb = sb("wr_sb", [P, KD, EXPERTS], F32)
        br_sb = sb("br_sb", [1, EXPERTS], F32)
        colsum = sb("colsum", [P, KD, CHUNKS], F32)
        misplaced = sb("misplaced", [1, 1], I32)
        route = sb("route", [1, 32, EXPERTS], F32)
        chosen = sb("chosen", [1, TOPK], I32)
        msum = sb("msum", [P, KD], F32)
        mixw = sb("mixw", [P, TOPK], F32)
        b1_sb = sb("b1_sb", [P, TOPK, KF], F32)
        b2_sb = sb("b2_sb", [P, TOPK, D], F32)
        b2mix = sb("b2mix", [P, D], F32)

        early = ExitStack()
        rows = sb("rows", [P, ITER, D], F32, early)
        rowsn = sb("rowsn", [P, ITER, D], F32, early)
        onehot = sb("onehot", [P, ITER, WIN], F32, early)
        onehot_wide = onehot[:, :, :].rearrange("p t w -> p (t w)").rearrange("p (s w) -> p s w", s=2)
        src_raw = sb("src_raw", [P, ROWCH + 1, P], I32, early)
        dst_raw = sb("dst_raw", [P, ROWCH + 1, P], I32, early)
        w_raw = sb("w_raw", [P, ROWCH + 1, P], F32, early)
        src_f = sb("src_f", [P, ROWCH + 1, P], F32, early)
        dst_f = sb("dst_f", [P, ROWCH + 1, P], F32, early)
        src_id = sb("src_id", [P, TILES + ITER], U32, early)
        dst_id = sb("dst_id", [P, TILES], F32, early)
        w_e = sb("w_e", [P, TILES], F32, early)
        base_i = sb("base_i", [1, TILES // GROUP], I32, early)
        dst_off = sb("dst_off", [P, TILES], F32, early)
        far = sb("far", [P, 3], F32, early)
        slot_id = sb("slot_id", [P, ITER], U32, early)
        iota_i = sb("iota_i", [P, WIDE], I32, early)
        iota = sb("iota", [P, WIDE], F32, early)
        stats = sb("stats", [P, 2, HALF, 6], F32, early)
        small = sb("small", [P, 2, 8, HALF], F32, early)
        dst_wide = sb("dst_wide", [P, HALF], F32, early)
        stage = sb("stage", [P, 2, KD, P], F32, early)
        xn = sb("xn", [P, 2, D], F32, early)
        nstats = sb("nstats", [P, 2, 6], F32, early)
        nsmall = sb("nsmall", [P, 6, 2], F32, early)
        early.close()

        w1h = sb("w1h", [P, TOPK, KD, FF], F32R)
        w1l = sb("w1l", [P, TOPK, KD, FF], F32R)
        w2h = sb("w2h", [P, TOPK, KF, D], F32R)
        w2l = sb("w2l", [P, TOPK, KF, D], F32R)
        staging = ExitStack()
        w1_raw = sb("w1_raw", [P, TOPK, KD, FF], F32, staging)
        w2_raw = sb("w2_raw", [P, TOPK, KF, D], F32, staging)
        staging.close()
        hh = sb("hh", [P, 2, HT, CHW], F32R)
        hl = sb("hl", [P, 2, HT, CHW], F32R)
        xh = sb("xh", [P, 2, KD, CHW], F32R)
        xl = sb("xl", [P, 2, KD, CHW], F32R)
        gel = sb("gel", [P, 2, 2, CHW], F32)
        z = sb("z", [P, 2, CH, D], F32)
        zn = sb("zn", [P, 2, CH, D], F32)
        zskip = sb("zskip", [P, 2, CH, D], F32)
        zstats = sb("zstats", [P, 2, CH, 6], F32)
        zsmall = sb("zsmall", [P, 2, 8, CH], F32)
        minus_half = sb("minus_half", [P, CH], F32)

        ps = ctx.enter_context(nc.psum_tensor("ps", [P, 8, 512], F32))
        psf = ps[:, :, :].rearrange("p b n -> p (b n)")

        src_in, dst_in, w_in, consts_in, x_in = (sem(n) for n in ("src_in", "dst_in", "w_in", "consts_in", "x_in"))
        pool_init, ident_ready, iota_ready = sem("pool_init"), sem("ident_ready"), sem("iota_ready")
        dve_init = sem("dve_init")
        src_float, src_turned, dst_float, dst_turned = (sem(n) for n in ("src_float", "src_turned", "dst_float", "dst_turned"))
        w_turned, dst_kept, base_spread, far_ready, far_summed = (
            sem(n) for n in ("w_turned", "dst_kept", "base_spread", "far_ready", "far_summed"))
        src_ready, path_known, setup_done = sem("src_ready"), sem("path_known"), sem("setup_done")
        turns = {e: sem(f"turns_{e}") for e in ("pool", "dve", "pe")}
        chain = sem("chain")
        ids_ready = sem("ids_ready")
        gathered = [sem(f"gathered{k}") for k in range(2 * GROUPS)]
        step_dve = sem("step_dve")
        var_ready, std_ready, scale_ready = sem("var_ready"), sem("std_ready"), sem("scale_ready")
        group_normed, onehot_ready = sem("group_normed"), sem("onehot_ready")
        half_free, sums_free, group_summed = sem("half_free"), sem("sums_free"), sem("group_summed")
        scale_step = sem("scale_step")
        wide_hot, wide_hot_free, wide_summed, wide_free, wide_step = (
            sem(n) for n in ("wide_hot", "wide_hot_free", "wide_summed", "wide_free", "wide_step"))
        edges_done = sem("edges_done")
        staged, stage_used, y_ready, y_used, x1_ready = (
            sem(n) for n in ("staged", "stage_used", "y_ready", "y_used", "x1_ready"))
        nstep, nvar, nstd, xn_ready, xn_turned, turned_free, xnT_ready = (
            sem(n) for n in ("nstep", "nvar", "nstd", "xn_ready", "xn_turned", "turned_free", "xnT_ready"))
        msum_ready, logits_ready, exp_in, exp_out, experts_known, mix_spread = (
            sem(n) for n in ("msum_ready", "logits_ready", "exp_in", "exp_out", "experts_known", "mix_spread"))
        w1_in, w2_in, b_in, w1_split, w2_split, raw_used = (
            sem(n) for n in ("w1_in", "w2_in", "b_in", "w1_split", "w2_split", "raw_used"))
        b_ready = sem("b_ready")
        xsplit_h, xsplit, xsplit_free, l1_done, l1_free, gelu_done, gelu_free = (
            sem(n) for n in ("xsplit_h", "xsplit", "xsplit_free", "l1_done", "l1_free", "gelu_done", "gelu_free"))
        hsplit_h, hsplit, h_free, l2_done, l2_free = (
            sem(n) for n in ("hsplit_h", "hsplit", "h_free", "l2_done", "l2_free"))
        zstep, zvar, zrstd, zscale, zn_done, zpool, out_ready, z_free = (
            sem(n) for n in ("zstep", "zvar", "zrstd", "zscale", "zn_done", "zpool", "out_ready", "z_free"))
        stored = sem("stored")

        def hold(eng, name, s, value):
            eng.wait_ge(s, value)
            eng.sem_inc(turns[name], 1)

        block = ctx.enter_context(nc.Block())

        last_edges = slice(EDGES - P, EDGES)

        def edge_rows(a):
            return a[0:FULL * P].rearrange("(t e) -> t e", e=P)

        @block.sync
        def _(sp):
            def load_edges(raw, a, s):
                sp.dma_start(raw[:, 0:ROWCH, :],
                             edge_rows(a)[0:ROWCH * P, :].rearrange("(c t) e -> t c e", c=ROWCH)).then_inc(s, 16)
                sp.dma_start(raw[0:ROWREST, ROWCH, :], edge_rows(a)[ROWCH * P:FULL, :]).then_inc(s, 16)
                for r in range(ROWREST, ROWTAIL):
                    sp.dma_start(raw[r:r + 1, ROWCH, :], a[last_edges].rearrange("(o e) -> o e", o=1)).then_inc(s, 16)
            load_edges(src_raw, src, src_in)
            load_edges(dst_raw, dst, dst_in)
            load_edges(w_raw, edge_w, w_in)
            sp.dma_start(gnnw_sb[:, :, :], gnn_w.rearrange("(k p) n -> p k n", k=KD)).then_inc(consts_in, 16)
            sp.dma_start(wr_sb[:, :, :], wr.rearrange("(k p) n -> p k n", k=KD)).then_inc(consts_in, 16)
            sp.dma_start(br_sb[:, :], br.rearrange("(o e) -> o e", o=1)).then_inc(consts_in, 16)
            sp.dma_start(gamma_bc[:, :], gamma.rearrange("(o e) -> o e", o=1).to_broadcast([P, D])).then_inc(consts_in, 16)
            sp.dma_start(beta_bc[:, :], beta.rearrange("(o e) -> o e", o=1).to_broadcast([P, D])).then_inc(consts_in, 16)
            sp.wait_ge(dve_init, 1)
            sp.dma_start(x1[:, 0:NFULL, :], x[0:NFULL * P, :].rearrange("(n p) d -> p n d", p=P)).then_inc(x_in, 16)
            sp.dma_start(x1[0:NREST, NFULL, :], x[NFULL * P:NODES, :]).then_inc(x_in, 16)
            sp.wait_ge(experts_known, 1)
            ids = [sp.value_load(chosen[0:1, e:e + 1], min_val=0, max_val=EXPERTS - 1) for e in range(TOPK)]
            for e in range(TOPK):
                sp.dma_start(w1_raw[:, e, :, :],
                             w1[bass.ds(ids[e], 1), :, :].rearrange("o (k p) f -> p (o k) f", k=KD)).then_inc(w1_in, 16)
            for e in range(TOPK):
                sp.dma_start(b1_sb[:, e, :],
                             b1[bass.ds(ids[e], 1), :].rearrange("o (t p) -> p (o t)", p=P),
                             allow_slow_non_contiguous=True).then_inc(b_in, 16)
                sp.dma_start(b2_sb[:, e, :], b2[bass.ds(ids[e], 1), :].to_broadcast([P, D])).then_inc(b_in, 16)
            for e in range(TOPK):
                sp.dma_start(w2_raw[:, e, :, :],
                             w2[bass.ds(ids[e], 1), :, :].rearrange("o (t p) d -> p (o t) d", t=KF)).then_inc(w2_in, 16)

            def store(c, par):
                sp.wait_ge(out_ready, c + 1)
                sp.dma_start(out[bass.ds(c * CHW, CHW), :].rearrange("(j p) d -> p j d", j=CH),
                             zn[:, par, :, :]).then_inc(stored, 16)
                sp.wait_ge(stored, 16 * (c + 1))
                sp.sem_inc(z_free, 1)
            sp.sem_inc(z_free, 2)
            with sp.Fori(0, CHUNKS // 2) as i:
                store(2 * i, 0)
                store(2 * i + 1, 1)
            sp.wait_ge(out_ready, CHUNKS)
            sp.dma_start(out[NFULL * P:NODES, :], zn[0:NREST, 0, 0, :]).then_inc(stored, 16)
            sp.wait_ge(stored, 16 * CHUNKS)

        @block.gpsimd
        def _(pool):
            nc.gpsimd.memset(ident[:, :], 0.0).then_inc(pool_init, 1)
            pool.wait_ge(pool_init, 1)
            nc.gpsimd.affine_select(out=ident[:, :], in_=ident[:, :], compare_op=ALU.not_equal, fill=1.0, base=0,
                                    pattern=[[-1, P]], channel_multiplier=1).then_inc(ident_ready, 1)
            nc.gpsimd.iota(iota_i[:, :], [[1, WIDE]], base=0, channel_multiplier=0).then_inc(iota_ready, 1)

            with pool.Fori(0, ITERS) as it:
                for h in range(2):
                    hold(pool, "pool", ids_ready, 2 * it + h + 1)
                    for t in range(h * HALF, (h + 1) * HALF):
                        nc.gpsimd.indirect_dma_start(
                            rows[:, t, :], None, x[:, :],
                            bass.IndirectOffsetOnAxis(ap=slot_id[:, t:t + 1], axis=0)).then_inc(gathered[t // GROUP], 16)

            pool.wait_ge(edges_done, 1)
            with pool.Fori(0, CHUNKS) as c:
                for j in range(CH):
                    pool.wait_ge(stage_used, 2 * c + j + 1)
                    nc.gpsimd.tensor_copy(stage[:, j, :, :],
                                          aggT[:, :, bass.ds((CH * c + j) * P, P)]).then_inc(staged, 1)

            pool.wait_ge(experts_known, 1)
            nc.gpsimd.memset(minus_half[:, :], -0.5).then_inc(pool_init, 1)
            pool.wait_ge(pool_init, 2)

            def split_x(c, par):
                pool.wait_ge(xsplit_free, c + 1)
                src_ = aggT[:, :, bass.ds(c * CHW, CHW)]
                nc.gpsimd.tensor_copy(xh[:, par, :, :], src_).then_inc(xsplit_h, 1)
                hold(pool, "pool", xsplit_h, c + 1)
                nc.gpsimd.tensor_tensor(xl[:, par, :, :], src_, xh[:, par, :, :].bitcast(F32),
                                        ALU.subtract).then_inc(xsplit, 1)

            def finish(c, par):
                pool.wait_ge(zvar, c + 1)
                nc.gpsimd.tensor_tensor(zsmall[:, par, 5, :], zsmall[:, par, 4, :], minus_half[:, :],
                                        ALU.pow).then_inc(zrstd, 1)
                x1c = x1[:, bass.ds(c * CH, CH), :]
                nc.gpsimd.tensor_tensor(zskip[:, par, :, :], x1c,
                                        beta_bc[:, :].unsqueeze(1).to_broadcast([P, CH, D]), ALU.add)
                pool.wait_ge(zn_done, c + 1)
                nc.gpsimd.tensor_tensor(zn[:, par, :, :], zn[:, par, :, :],
                                        gamma_bc[:, :].unsqueeze(1).to_broadcast([P, CH, D]), ALU.mult).then_inc(zpool, 1)
                pool.wait_ge(zpool, c + 1)
                nc.gpsimd.tensor_tensor(zn[:, par, :, :], zn[:, par, :, :], zskip[:, par, :, :],
                                        ALU.add).then_inc(out_ready, 1)

            split_x(0, 0)
            split_x(1, 1)
            with pool.Fori(0, CHUNKS // 2) as i:
                split_x(2 * i + 2, 0)
                finish(2 * i, 0)
                split_x(2 * i + 3, 1)
                finish(2 * i + 1, 1)
            finish(CHUNKS - 1, 0)

        @block.scalar
        def _(act):
            act.wait_ge(src_ready, 1)
            for h in range(2):
                nc.scalar.copy(slot_id[:, h * HALF:(h + 1) * HALF],
                               src_id[:, h * HALF:(h + 1) * HALF]).then_inc(ids_ready, 1)
            act.wait_ge(setup_done, 1)
            with act.Fori(0, ITERS) as it:
                for h in range(2):
                    n = 2 * it + h
                    act.wait_ge(var_ready, n + 1)
                    nc.scalar.activation(small[:, h, 4, :], small[:, h, 3, :], ACT.Sqrt, bias=epsc[:, 0:1],
                                         scale=1.0 / D).then_inc(std_ready, 1)
                    act.wait_ge(scale_ready, n + 1)
                    act.wait_ge(half_free, n + 1)
                    for t in range(HALF):
                        i = nc.scalar.activation(rowsn[:, h * HALF + t, :], rows[:, h * HALF + t, :], ACT.Identity,
                                                 bias=small[:, h, 7, t:t + 1], scale=small[:, h, 6, t:t + 1])
                        if t % GROUP == GROUP - 1:
                            i.then_inc(group_normed, 1)
                    act.wait_ge(group_normed, GROUPS * (n + 1))
                    nc.scalar.copy(slot_id[:, h * HALF:(h + 1) * HALF],
                                   src_id[:, bass.ds(ITER * (it + 1) + h * HALF, HALF)]).then_inc(ids_ready, 1)

            act.sem_inc(xnT_ready, KD)
            with act.Fori(0, CHUNKS) as c:
                act.wait_ge(nvar, c + 1)
                nc.scalar.activation(nsmall[:, 4, :], nsmall[:, 3, :], ACT.Sqrt, bias=epsc[:, 0:1],
                                     scale=1.0 / D).then_inc(nstd, 1)
                act.wait_ge(xn_turned, c + 2)
                for k in range(KD):
                    nc.scalar.activation(aggT[:, k, bass.ds(c * CHW, CHW)].rearrange("p (j n) -> p j n", j=CH),
                                         ps[:, 4 + k, 0:CHW].rearrange("p (j n) -> p j n", j=CH),
                                         ACT.Identity, accum_out=colsum[:, k, bass.ds(c, 1)]).then_inc(xnT_ready, 1)
            for n, (o, i, b) in enumerate(((2, 1, 31), (8, 7, 30))):
                act.wait_ge(exp_in, n + 1)
                nc.scalar.activation(route[0:1, o, :], route[0:1, i, :], ACT.Exp,
                                     bias=route[0:1, b, 0:1]).then_inc(exp_out, 1)
            act.wait_ge(exp_in, 3)
            nc.scalar.activation(route[0:1, 22, 0:1], route[0:1, 21, 0:1], ACT.Exp).then_inc(exp_out, 1)

            act.wait_ge(b_in, 16 * 2 * TOPK)

            def gelu(c):
                for q in range(PAIRS):
                    act.wait_ge(l1_done, PAIRS * c + q + 1)
                    act.wait_ge(gelu_free, PAIRS * c + q + 1)
                    for s in range(2):
                        f = 2 * q + s
                        i = nc.scalar.activation(gel[:, q % 2, s, :], ps[:, q, s * CHW:(s + 1) * CHW], ACT.Gelu,
                                                 bias=b1_sb[:, f // KF, f % KF:f % KF + 1])
                    i.then_inc(gelu_done, 1)

            def norm(c, par):
                act.wait_ge(zscale, c + 1)
                act.wait_ge(z_free, c + 1)
                for j in range(CH):
                    i = nc.scalar.activation(zn[:, par, j, :], z[:, par, j, :], ACT.Identity,
                                             bias=zsmall[:, par, 6, j:j + 1], scale=zsmall[:, par, 5, j:j + 1])
                i.then_inc(zn_done, 1)

            gelu(0)
            with act.Fori(0, CHUNKS // 2) as i:
                for s in range(2):
                    gelu(2 * i + 1 + s)
                    norm(2 * i + s, s)
            norm(CHUNKS - 1, 0)

        @block.vector
        def _(dve):
            done = [0]

            def link(ins):
                done[0] += 1
                ins.then_inc(chain, 1)
                dve.wait_ge(chain, done[0])

            nc.vector.memset(x1[:, NFULL:NT, :], 0.0).then_inc(dve_init, 1)
            nc.vector.memset(epsc[:, :], EPS)
            link(nc.vector.memset(ones[:, :], 1.0))
            dve.wait_ge(src_in, 16 * (2 + ROWTAIL - ROWREST))
            nc.vector.tensor_copy(src_f[:, 0:ROWCH, :], src_raw[:, 0:ROWCH, :])
            nc.vector.tensor_copy(src_f[0:ROWTAIL, ROWCH, :], src_raw[0:ROWTAIL, ROWCH, :]).then_inc(src_float, 1)
            nc.vector.memset(src_id[:, TILES:TILES + ITER], 0)
            dve.wait_ge(dst_in, 16 * (2 + ROWTAIL - ROWREST))
            nc.vector.tensor_copy(dst_f[:, 0:ROWCH, :], dst_raw[:, 0:ROWCH, :])
            nc.vector.tensor_copy(dst_f[0:ROWTAIL, ROWCH, :], dst_raw[0:ROWTAIL, ROWCH, :]).then_inc(dst_float, 1)
            dve.wait_ge(src_turned, 1)
            nc.vector.tensor_copy(src_id[:, 0:TILES], psf[:, 0:TILES]).then_inc(src_ready, 1)
            dve.wait_ge(dst_turned, 1)
            nc.vector.tensor_copy(dst_id[:, :], psf[:, 1024:1024 + TILES]).then_inc(dst_kept, 1)
            dve.wait_ge(iota_ready, 1)
            nc.vector.tensor_copy(iota[:, :], iota_i[:, :])
            dve.wait_ge(w_turned, 1)
            link(nc.vector.tensor_copy(w_e[:, :], psf[:, 2048:2048 + TILES]))
            nc.vector.memset(w_e[:, FULL + 1:TILES], 0.0)
            nc.vector.memset(w_e[0:P - LEFT, FULL:FULL + 1], 0.0)
            dve.wait_ge(base_spread, 1)
            nc.vector.tensor_copy(base_i[0:1, :], psf[0:1, 3072:3072 + TILES // GROUP])
            link(nc.vector.tensor_tensor(dst_off[:, :].rearrange("p (g t) -> p g t", t=GROUP),
                                         dst_id[:, :].rearrange("p (g t) -> p g t", t=GROUP),
                                         psf[:, 3072:3072 + TILES // GROUP].unsqueeze(2).to_broadcast([P, TILES // GROUP, GROUP]),
                                         ALU.subtract))
            nc.vector.tensor_reduce(far[:, 0:1], dst_off[:, :], AX.X, ALU.max)
            link(nc.vector.tensor_reduce(far[:, 1:2], dst_off[:, :], AX.X, ALU.min, negate=True))
            link(nc.vector.tensor_scalar(far[:, 2:3], far[:, 1:2], float(WIN - 1), far[:, 0:1], ALU.add, ALU.max))
            nc.vector.tensor_scalar(far[:, 2:3], far[:, 2:3], float(WIN - 1), None, ALU.is_gt).then_inc(far_ready, 1)
            dve.wait_ge(far_summed, 1)
            nc.vector.tensor_copy(misplaced[0:1, 0:1], psf[0:1, 3584:3585]).then_inc(path_known, 1)
            dve.wait_ge(path_known, 1)
            nc.vector.memset(aggT[:, :, :], 0.0).then_inc(setup_done, 1)
            dve.wait_ge(setup_done, 1)

            LINKS = 4

            def row_stats(it, h):
                n = 2 * it + h
                for t in range(HALF):
                    if t % GROUP == 0:
                        dve.wait_ge(gathered[h * GROUPS + t // GROUP], 16 * GROUP * (it + 1))
                    i = nc.vector.bn_stats(stats[:, h, t, :], rows[:, h * HALF + t, :])
                i.then_inc(step_dve, 1)
                dve.wait_ge(step_dve, LINKS * n + 1)
                st = stats[:, h, :, :]
                sm = small[:, h, :, :]
                nc.vector.tensor_tensor(sm[:, 0, :], st[:, :, 1], st[:, :, 4], ALU.add)
                nc.vector.tensor_tensor(sm[:, 2, :], st[:, :, 2], st[:, :, 5], ALU.add)
                nc.vector.tensor_tensor(sm[:, 1, :], st[:, :, 1], st[:, :, 4], ALU.subtract).then_inc(step_dve, 1)
                dve.wait_ge(step_dve, LINKS * n + 2)
                nc.vector.scalar_tensor_tensor(sm[:, 5, :], sm[:, 1, :], D / 4.0, sm[:, 1, :], ALU.mult,
                                               ALU.mult).then_inc(step_dve, 1)
                dve.wait_ge(step_dve, LINKS * n + 3)
                nc.vector.tensor_tensor(sm[:, 3, :], sm[:, 5, :], sm[:, 2, :], ALU.add).then_inc(var_ready, 1)

            def row_scale(it, h):
                n = 2 * it + h
                sm = small[:, h, :, :]
                dve.wait_ge(std_ready, n + 1)
                nc.vector.reciprocal(sm[:, 5, :], sm[:, 4, :]).then_inc(step_dve, 1)
                dve.wait_ge(step_dve, LINKS * n + 4)
                nc.vector.tensor_tensor(sm[:, 6, :], sm[:, 5, :], w_e[:, bass.ds(ITER * it + HALF * h, HALF)],
                                        ALU.mult).then_inc(scale_step, 1)
                dve.wait_ge(scale_step, n + 1)
                nc.vector.scalar_tensor_tensor(sm[:, 7, :], sm[:, 0, :], -0.5, sm[:, 6, :], ALU.mult,
                                               ALU.mult).then_inc(scale_ready, 1)

            def hot(it, h):
                n = 2 * it + h
                dve.wait_ge(half_free, n + 1)
                off = dst_off[:, bass.ds(ITER * it + HALF * h, HALF)]
                nc.vector.tensor_tensor(onehot[:, h * HALF:(h + 1) * HALF, :],
                                        iota[:, 0:WIN].unsqueeze(1).to_broadcast([P, HALF, WIN]),
                                        off.unsqueeze(2).to_broadcast([P, HALF, WIN]),
                                        ALU.is_equal).then_inc(onehot_ready, 1)

            def add_sums(it, h):
                n = 2 * it + h
                for g in range(GROUPS):
                    base = dve.value_load(base_i[0:1, bass.ds(2 * GROUPS * it + GROUPS * h + g, 1)],
                                          min_val=0, max_val=NODES - 1)
                    win = aggT[:, :, bass.ds(base, WIN)]
                    dve.wait_ge(group_summed, GROUPS * n + g + 1)
                    nc.vector.tensor_tensor(win, win,
                                            ps[:, h * GROUPS + g, 0:KD * WIN].rearrange("p (k m) -> p k m", k=KD),
                                            ALU.add).then_inc(sums_free, 1)
                    dve.wait_ge(sums_free, GROUPS * n + g + 1)

            path = dve.value_load(misplaced[0:1, 0:1], min_val=0, max_val=P)
            with dve.If(path == 0):
                row_stats(0, 0)
                row_scale(0, 0)
                hot(0, 0)
                with dve.Fori(0, ITERS - 1) as it:
                    row_stats(it, 1)
                    row_scale(it, 1)
                    hot(it, 1)
                    add_sums(it, 0)
                    row_stats(it + 1, 0)
                    row_scale(it + 1, 0)
                    hot(it + 1, 0)
                    add_sums(it, 1)
                row_stats(ITERS - 1, 1)
                row_scale(ITERS - 1, 1)
                hot(ITERS - 1, 1)
                add_sums(ITERS - 1, 0)
                add_sums(ITERS - 1, 1)
            with dve.Else():
                dve.sem_inc(wide_free, 1)
                with dve.Fori(0, ITERS) as it:
                    for h in range(2):
                        n = 2 * it + h
                        row_stats(it, h)
                        row_scale(it, h)
                        nc.vector.tensor_copy(dst_wide[:, :], dst_id[:, bass.ds(ITER * it + HALF * h, HALF)]).then_inc(wide_step, 1)
                        hold(dve, "dve", wide_step, n * (2 * WIDES + 1) + 1)
                        with dve.Fori(0, WIDES) as v:
                            for t in range(HALF):
                                dve.wait_ge(wide_hot_free, HALF * (WIDES * n + v) + t + 1)
                                nc.vector.tensor_scalar(onehot_wide[:, t % 2, :], iota[:, :], dst_wide[:, t:t + 1], None,
                                                        ALU.is_equal).then_inc(wide_hot, 1)
                            dve.wait_ge(wide_hot, HALF * (WIDES * n + v + 1))
                            nc.vector.tensor_scalar(dst_wide[:, :], dst_wide[:, :], float(-WIDE), None,
                                                    ALU.add).then_inc(wide_step, 1)
                            dve.wait_ge(wide_step, n * (2 * WIDES + 1) + 2 * v + 2)
                            win = aggT[:, :, bass.ds(v * WIDE, WIDE)]
                            dve.wait_ge(wide_summed, WIDES * n + v + 1)
                            nc.vector.tensor_tensor(win, win, ps[:, 0:KD, :], ALU.add).then_inc(wide_step, 1)
                            dve.wait_ge(wide_step, n * (2 * WIDES + 1) + 2 * v + 3)
                            dve.sem_inc(wide_free, 1)

            dve.sem_inc(edges_done, 1)
            dve.wait_ge(x_in, 32)
            with dve.Fori(0, CHUNKS) as c:
                for j in range(CH):
                    tile_ = x1[:, bass.ds(CH * c + j, 1), :].rearrange("p o d -> p (o d)")
                    dve.wait_ge(y_ready, 2 * c + j + 1)
                    nc.vector.scalar_tensor_tensor(tile_, ps[:, j, 0:D], 0.0, tile_, ALU.max, ALU.add).then_inc(x1_ready, 1)
                    hold(dve, "dve", x1_ready, 2 * c + j + 1)
                    i = nc.vector.bn_stats(nstats[:, j, :], tile_)
                i.then_inc(nstep, 1)
                dve.wait_ge(nstep, 4 * c + 1)
                nc.vector.tensor_tensor(nsmall[:, 0, :], nstats[:, :, 1], nstats[:, :, 4], ALU.add)
                nc.vector.tensor_tensor(nsmall[:, 2, :], nstats[:, :, 2], nstats[:, :, 5], ALU.add)
                nc.vector.tensor_tensor(nsmall[:, 1, :], nstats[:, :, 1], nstats[:, :, 4], ALU.subtract).then_inc(nstep, 1)
                dve.wait_ge(nstep, 4 * c + 2)
                nc.vector.scalar_tensor_tensor(nsmall[:, 5, :], nsmall[:, 1, :], D / 4.0, nsmall[:, 1, :], ALU.mult,
                                               ALU.mult).then_inc(nstep, 1)
                dve.wait_ge(nstep, 4 * c + 3)
                nc.vector.tensor_tensor(nsmall[:, 3, :], nsmall[:, 5, :], nsmall[:, 2, :], ALU.add).then_inc(nvar, 1)
                dve.wait_ge(nstd, c + 1)
                r = rstd1[:, bass.ds(CH * c, CH)]
                s = shift1[:, bass.ds(CH * c, CH)]
                nc.vector.reciprocal(nsmall[:, 5, :], nsmall[:, 4, :]).then_inc(nstep, 1)
                dve.wait_ge(nstep, 4 * c + 4)
                nc.vector.tensor_copy(r, nsmall[:, 5, :])
                nc.vector.scalar_tensor_tensor(nsmall[:, 1, :], nsmall[:, 0, :], -0.5, nsmall[:, 5, :], ALU.mult,
                                               ALU.mult).then_inc(y_used, 1)
                dve.wait_ge(y_used, c + 1)
                nc.vector.tensor_copy(s, nsmall[:, 1, :])
                dve.wait_ge(xn_turned, c + 1)
                for j in range(CH):
                    tile_ = x1[:, bass.ds(CH * c + j, 1), :].rearrange("p o d -> p (o d)")
                    i = nc.vector.tensor_scalar(xn[:, j, :], tile_, nsmall[:, 5, j:j + 1], nsmall[:, 1, j:j + 1],
                                                ALU.mult, ALU.add)
                i.then_inc(xn_ready, 1)

            R = lambda k: route[0:1, k, :]
            S = lambda k: route[0:1, k, 0:1]
            dve.wait_ge(xnT_ready, KD * (CHUNKS + 1))
            nc.vector.tensor_reduce(msum[:, :], colsum[:, :, :], AX.X, ALU.add).then_inc(msum_ready, 1)
            dve.wait_ge(iota_ready, 1)
            link(nc.vector.tensor_copy(R(15), iota[0:1, 0:EXPERTS]))
            link(nc.vector.tensor_scalar(R(16), R(15), float(EXPERTS), None, ALU.add))
            dve.wait_ge(consts_in, 16 * 5)
            dve.wait_ge(logits_ready, 1)
            link(nc.vector.scalar_tensor_tensor(R(1), ps[0:1, 6, 0:EXPERTS], 1.0 / NODES, br_sb[0:1, :],
                                                ALU.mult, ALU.add))

            def softmax(n, logit, shift, ex, res):
                nc.vector.tensor_reduce(S(shift), R(logit), AX.X, ALU.max, negate=True).then_inc(exp_in, 1)
                dve.wait_ge(exp_out, n + 1)
                link(nc.vector.reduce_sum(S(29), R(ex), AX.X))
                link(nc.vector.reciprocal(S(28), S(29)))
                link(nc.vector.tensor_scalar(R(res), R(ex), S(28), None, ALU.mult))
            softmax(0, 1, 31, 2, 3)
            link(nc.vector.tensor_scalar(R(4), R(3), float(NODES), 1.0, ALU.mult, ALU.max))
            link(nc.vector.reciprocal(R(5), R(4)))
            link(nc.vector.tensor_scalar(R(6), R(5), CAPACITY, 1.0, ALU.mult, ALU.min))
            link(nc.vector.tensor_tensor(R(7), R(3), R(6), ALU.mult))
            softmax(1, 7, 30, 8, 9)
            value = 9
            for e in range(TOPK):
                link(nc.vector.tensor_reduce(S(17 + e), R(value), AX.X, ALU.max))
                link(nc.vector.tensor_scalar(R(10), R(value), S(17 + e), None, ALU.is_equal))
                link(nc.vector.scalar_tensor_tensor(R(11), R(10), -float(EXPERTS), R(16), ALU.mult, ALU.add))
                link(nc.vector.tensor_reduce(S(19 + e), R(11), AX.X, ALU.min))
                link(nc.vector.tensor_copy(chosen[0:1, e:e + 1], S(19 + e)))
                if e == 0:
                    link(nc.vector.tensor_scalar(R(12), R(15), S(19), None, ALU.is_equal))
                    link(nc.vector.scalar_tensor_tensor(R(13), R(12), -2.0, R(9), ALU.mult, ALU.add))
                    value = 13
            dve.sem_inc(experts_known, 1)
            nc.vector.tensor_tensor(S(21), S(18), S(17), ALU.subtract).then_inc(exp_in, 1)
            dve.wait_ge(exp_out, 3)
            link(nc.vector.tensor_scalar(S(23), S(22), 1.0, None, ALU.add))
            link(nc.vector.reciprocal(route[0:1, 24, 0:1], S(23)))
            nc.vector.tensor_tensor(route[0:1, 24, 1:2], S(22), route[0:1, 24, 0:1], ALU.mult).then_inc(mix_spread, 1)
            dve.wait_ge(mix_spread, 2)
            link(nc.vector.tensor_copy(mixw[:, :], ps[:, 7, 0:TOPK]))

            dve.sem_inc(gelu_free, 2)
            dve.sem_inc(l2_free, 2)
            dve.wait_ge(w1_in, 16 * TOPK)
            link(nc.vector.tensor_copy(w1h[:, :, :, :], w1_raw[:, :, :, :]))
            nc.vector.tensor_tensor(w1l[:, :, :, :], w1_raw[:, :, :, :], w1h[:, :, :, :].bitcast(F32),
                                    ALU.subtract).then_inc(w1_split, 1)
            dve.wait_ge(b_in, 16 * 2 * TOPK)
            link(nc.vector.tensor_scalar(b2mix[:, :], b2_sb[:, 0, :], mixw[:, 0:1], None, ALU.mult))
            link(nc.vector.scalar_tensor_tensor(b2mix[:, :], b2_sb[:, 1, :], mixw[:, 1:2], b2mix[:, :], ALU.mult, ALU.add))
            dve.wait_ge(w2_in, 16 * TOPK)
            for e in range(TOPK):
                link(nc.vector.tensor_scalar(w2h[:, e, :, :], w2_raw[:, e, :, :], mixw[:, e:e + 1], None, ALU.mult))
                link(nc.vector.scalar_tensor_tensor(w2l[:, e, :, :].rearrange("p t d -> p (t d)"),
                                                    w2_raw[:, e, :, :].rearrange("p t d -> p (t d)"), mixw[:, e:e + 1],
                                                    w2h[:, e, :, :].rearrange("p t d -> p (t d)").bitcast(F32),
                                                    ALU.mult, ALU.subtract))
            dve.sem_inc(w2_split, 1)

            def split_h(c, par):
                dve.wait_ge(h_free, c + 1)
                for q in range(PAIRS):
                    dve.wait_ge(gelu_done, PAIRS * c + q + 1)
                    nc.vector.tensor_copy(hh[:, par, 2 * q:2 * q + 2, :], gel[:, q % 2, :, :]).then_inc(hsplit_h, 1)
                    dve.wait_ge(hsplit_h, PAIRS * c + q + 1)
                    nc.vector.tensor_tensor(hl[:, par, 2 * q:2 * q + 2, :], gel[:, q % 2, :, :],
                                            hh[:, par, 2 * q:2 * q + 2, :].bitcast(F32), ALU.subtract).then_inc(gelu_free, 1)
                dve.wait_ge(gelu_free, PAIRS * (c + 1) + 2)
                dve.sem_inc(hsplit, 1)

            ZL = 7

            def out_norm(c, par):
                sm = zsmall[:, par, :, :]
                for j in range(CH):
                    tile_ = x1[:, bass.ds(CH * c + j, 1), :].rearrange("p o d -> p (o d)")
                    nc.vector.scalar_tensor_tensor(z[:, par, j, :], tile_, rstd1[:, bass.ds(CH * c + j, 1)], b2mix[:, :],
                                                   ALU.mult, ALU.add).then_inc(zstep, 1)
                    dve.wait_ge(zstep, ZL * c + 2 * j + 1)
                    if j == 0:
                        dve.wait_ge(l2_done, c + 1)
                    nc.vector.scalar_tensor_tensor(z[:, par, j, :], ps[:, 4 + 2 * par + j, 0:D],
                                                   shift1[:, bass.ds(CH * c + j, 1)], z[:, par, j, :],
                                                   ALU.add, ALU.add).then_inc(zstep, 1)
                    dve.wait_ge(zstep, ZL * c + 2 * j + 2)
                    i = nc.vector.bn_stats(zstats[:, par, j, :], z[:, par, j, :])
                i.then_inc(l2_free, 1)
                dve.wait_ge(l2_free, c + 3)
                st = zstats[:, par, :, :]
                nc.vector.tensor_tensor(sm[:, 0, :], st[:, :, 1], st[:, :, 4], ALU.add)
                nc.vector.tensor_tensor(sm[:, 2, :], st[:, :, 2], st[:, :, 5], ALU.add)
                nc.vector.tensor_tensor(sm[:, 1, :], st[:, :, 1], st[:, :, 4], ALU.subtract).then_inc(zstep, 1)
                dve.wait_ge(zstep, ZL * c + 5)
                nc.vector.scalar_tensor_tensor(sm[:, 3, :], sm[:, 1, :], D / 4.0, sm[:, 1, :], ALU.mult,
                                               ALU.mult).then_inc(zstep, 1)
                dve.wait_ge(zstep, ZL * c + 6)
                nc.vector.tensor_tensor(sm[:, 7, :], sm[:, 3, :], sm[:, 2, :], ALU.add).then_inc(zstep, 1)
                dve.wait_ge(zstep, ZL * c + 7)
                nc.vector.tensor_scalar(sm[:, 4, :], sm[:, 7, :], 1.0 / D, EPS, ALU.mult, ALU.add).then_inc(zvar, 1)

            def out_scale(c, par):
                sm = zsmall[:, par, :, :]
                dve.wait_ge(zrstd, c + 1)
                nc.vector.scalar_tensor_tensor(sm[:, 6, :], sm[:, 0, :], -0.5, sm[:, 5, :], ALU.mult,
                                               ALU.mult).then_inc(zscale, 1)

            split_h(0, 0)
            with dve.Fori(0, CHUNKS // 2) as i:
                for s in range(2):
                    split_h(2 * i + 1 + s, 1 - s)
                    out_norm(2 * i + s, s)
                    out_scale(2 * i + s, s)
            out_norm(CHUNKS - 1, 0)
            out_scale(CHUNKS - 1, 0)

        @block.tensor
        def _(pe):
            def turn(dst_col, chunks, done_sem):
                for c in range(ROWCH):
                    nc.tensor.transpose(psf[:, dst_col + c * P:dst_col + (c + 1) * P], chunks[:, c, :], ident[:, :])
                nc.tensor.transpose(psf[:, dst_col + ROWCH * P:dst_col + TILES], chunks[0:ROWTAIL, ROWCH, :],
                                    ident[0:ROWTAIL, 0:ROWTAIL]).then_inc(done_sem, 1)
            pe.wait_ge(ident_ready, 1)
            pe.wait_ge(src_float, 1)
            turn(0, src_f, src_turned)
            pe.wait_ge(dst_float, 1)
            turn(1024, dst_f, dst_turned)
            pe.wait_ge(w_in, 16 * (2 + ROWTAIL - ROWREST))
            turn(2048, w_raw, w_turned)
            pe.wait_ge(dst_kept, 1)
            nc.tensor.matmul(psf[:, 3072:3072 + TILES // GROUP], ones[0:1, :],
                             dst_id[0:1, :].rearrange("p (g t) -> p g t", t=GROUP)[:, :, 0],
                             start=True, stop=True).then_inc(base_spread, 1)
            pe.wait_ge(far_ready, 1)
            nc.tensor.matmul(psf[0:1, 3584:3585], far[:, 2:3], ones[:, 0:1], start=True, stop=True).then_inc(far_summed, 1)
            pe.wait_ge(path_known, 1)
            pe.wait_ge(setup_done, 1)
            pe.sem_inc(half_free, 2)
            path = pe.value_load(misplaced[0:1, 0:1], min_val=0, max_val=P)

            def sum_half(it, h):
                n = 2 * it + h
                pe.wait_ge(onehot_ready, n + 1)
                for g in range(GROUPS):
                    pe.wait_ge(group_normed, GROUPS * n + g + 1)
                    for k in range(KD):
                        for t in range(GROUP):
                            slot = h * HALF + g * GROUP + t
                            i = nc.tensor.matmul(ps[:, h * GROUPS + g, k * WIN:(k + 1) * WIN],
                                                 rowsn[:, slot, k * P:(k + 1) * P], onehot[:, slot, :],
                                                 start=(t == 0), stop=(t == GROUP - 1))
                    i.then_inc(group_summed, 1)
                pe.wait_ge(group_summed, GROUPS * (n + 1))
                pe.sem_inc(half_free, 1)

            with pe.If(path == 0):
                sum_half(0, 0)
                sum_half(0, 1)
                with pe.Fori(1, ITERS) as it:
                    for h in range(2):
                        pe.wait_ge(sums_free, GROUPS * (2 * it + h - 1))
                        sum_half(it, h)
            with pe.Else():
                pe.sem_inc(wide_hot_free, 2)
                with pe.Fori(0, ITERS) as it:
                    for h in range(2):
                        n = 2 * it + h
                        hold(pe, "pe", group_normed, GROUPS * (n + 1))
                        with pe.Fori(0, WIDES) as v:
                            pe.wait_ge(wide_free, WIDES * n + v + 1)
                            for t in range(HALF):
                                pe.wait_ge(wide_hot, HALF * (WIDES * n + v) + t + 1)
                                for k in range(KD):
                                    i = nc.tensor.matmul(ps[:, k, :], rowsn[:, h * HALF + t, k * P:(k + 1) * P],
                                                         onehot_wide[:, t % 2, :], start=(t == 0), stop=(t == HALF - 1))
                                i.then_inc(wide_hot_free, 1)
                            pe.wait_ge(wide_hot_free, HALF * (WIDES * n + v + 1) + 2)
                            pe.sem_inc(wide_summed, 1)
                        pe.sem_inc(half_free, 1)

            pe.wait_ge(edges_done, 1)
            pe.wait_ge(consts_in, 16 * 5)
            pe.sem_inc(stage_used, 2)
            pe.sem_inc(xn_turned, 1)

            def project(c, first=False):
                for j in range(CH):
                    pe.wait_ge(staged, CH * c + j + 1)
                    if not first:
                        pe.wait_ge(x1_ready, CH * (c - 1) + j + 1)
                    for k in range(KD):
                        i = nc.tensor.matmul(ps[:, j, 0:D], stage[:, j, k, :], gnnw_sb[:, k, :],
                                             start=(k == 0), stop=(k == KD - 1))
                    i.then_inc(y_ready, 1)
                    pe.wait_ge(y_ready, CH * c + j + 1)
                    pe.sem_inc(stage_used, 1)

            def turn_xn(c):
                pe.wait_ge(xn_ready, c + 1)
                pe.wait_ge(xnT_ready, KD * (c + 1))
                for k in range(KD):
                    for j in range(CH):
                        i = nc.tensor.transpose(ps[:, 4 + k, j * P:(j + 1) * P], xn[:, j, k * P:(k + 1) * P], ident[:, :])
                i.then_inc(xn_turned, 1)

            project(0, True)
            with pe.Fori(0, CHUNKS - 1) as c:
                project(c + 1)
                turn_xn(c)
            turn_xn(CHUNKS - 1)

            pe.wait_ge(msum_ready, 1)
            for k in range(KD):
                i = nc.tensor.matmul(ps[0:1, 6, 0:EXPERTS], msum[:, k:k + 1], wr_sb[:, k, :],
                                     start=(k == 0), stop=(k == KD - 1))
            i.then_inc(logits_ready, 1)
            pe.wait_ge(mix_spread, 1)
            nc.tensor.matmul(ps[:, 7, 0:TOPK], ones[0:1, :], route[0:1, 24, 0:TOPK], start=True, stop=True).then_inc(mix_spread, 1)

            pe.sem_inc(xsplit_free, 2)
            pe.sem_inc(h_free, 2)
            pe.wait_ge(w1_split, 1)

            def layer1(c, par, first=False):
                pe.wait_ge(xsplit, c + 1)
                for q in range(PAIRS):
                    if not first:
                        pe.wait_ge(gelu_done, PAIRS * (c - 1) + q + 1)
                    for s in range(2):
                        f = 2 * q + s
                        e, ft = f // KF, f % KF
                        dst_ = ps[:, q, s * CHW:(s + 1) * CHW]
                        n = 0
                        for k in range(KD):
                            for w_, x_ in ((w1h, xh), (w1l, xh), (w1h, xl)):
                                i = nc.tensor.matmul(dst_, w_[:, e, k, ft * P:(ft + 1) * P], x_[:, par, k, :],
                                                     start=(n == 0), stop=(n == 3 * KD - 1))
                                n += 1
                    i.then_inc(l1_done, 1)
                pe.wait_ge(l1_done, PAIRS * (c + 1))
                pe.sem_inc(xsplit_free, 1)

            def layer2(c, par):
                pe.wait_ge(hsplit, c + 1)
                pe.wait_ge(l2_free, c + 1)
                for j in range(CH):
                    n = 0
                    for f in range(HT):
                        e, ft = f // KF, f % KF
                        for h_, w_ in ((hh, w2h), (hh, w2l), (hl, w2h)):
                            i = nc.tensor.matmul(ps[:, 4 + 2 * par + j, 0:D], h_[:, par, f, j * P:(j + 1) * P],
                                                 w_[:, e, ft, :], start=(n == 0), stop=(n == 3 * HT - 1))
                            n += 1
                i.then_inc(l2_done, 1)
                pe.wait_ge(l2_done, c + 1)
                pe.sem_inc(h_free, 1)

            layer1(0, 0, True)
            pe.wait_ge(w2_split, 1)
            with pe.Fori(0, CHUNKS // 2) as i_:
                for s in range(2):
                    layer1(2 * i_ + 1 + s, 1 - s)
                    layer2(2 * i_ + s, s)
            layer2(CHUNKS - 1, 0)


_INS = ["x", "src", "dst", "edge_weight", "L0_gnn_weight", "L0_ffn_Wr", "L0_ffn_br", "L0_ffn_W1", "L0_ffn_b1",
        "L0_ffn_W2", "L0_ffn_b2", "L0_ffn_gamma", "L0_ffn_beta"]


def kernel(**inputs):
    import numpy as _np
    import concourse.bacc as _bacc
    from concourse import mybir as _mybir
    from concourse.bass_utils import run_bass_kernel_spmd as _run

    nc = _bacc.Bacc("TRN2", target_bir_lowering=False, num_devices=1)
    arrays, args = {}, []
    for name in _INS:
        a = _np.ascontiguousarray(inputs[name])
        arrays[f"in_{name}"] = a
        args.append(nc.dram_tensor(f"in_{name}", a.shape, _mybir.dt.from_np(a.dtype), kind="ExternalInput").ap())
    result = nc.dram_tensor("out_0", (NODES, D), _mybir.dt.float32, kind="ExternalOutput").ap()
    gnn_moe(nc, *args, result)
    return _run(nc, [arrays], core_ids=[0]).results[0]["out_0"]
```
